# Optimizing a Trainium2 kernel written in Bass

```python
import numpy as np
import jax
import jax.numpy as jnp

def _softmax(x, axis=-1):
    return jax.nn.softmax(x, axis=axis)
def _gelu(x):
    return jax.nn.gelu(x, approximate=True)
def _silu(x):
    return jax.nn.silu(x)
def _sigmoid(x):
    return jax.nn.sigmoid(x)
def _layernorm(x, axis=-1, eps=1e-5):
    m = jnp.mean(x, axis=axis, keepdims=True)
    v = jnp.var(x, axis=axis, keepdims=True)
    return (x - m) / jnp.sqrt(v + eps)
def _scatter_add(tgt, idx, src, axis=0):
    return tgt.at[idx].add(src)
def _segment_sum(src, seg, n):
    return jax.ops.segment_sum(src, seg, n)

kernel_name = 'mk_conv_seq_d1_conv_nchw512_6cd7ee'

def setup_inputs(seed: int = 0):
    np.random.seed(seed)
    _w = jnp.asarray
    def _rec_inputs():
        import jax
        import jax.numpy as jnp
        _gk = jax.random.key(seed)
        x = -9.26e-05 + 0.9999 * jax.random.normal(jax.random.fold_in(_gk, 1), (8, 512, 96, 96), jnp.float32)
        return x
    x = _rec_inputs()
    def _L0_conv_setup():
        import jax, jax.numpy as jnp
        import numpy as np
        C = 512
        CQK = C // 8
        key = jax.random.key(seed)
        ks = jax.random.split(key, 8)
        x = jax.random.normal(ks[0], (8, C, 96, 96), dtype=jnp.float32)
        wq = jax.random.normal(ks[1], (CQK, C), dtype=jnp.float32) * 0.02
        bq = jnp.zeros((CQK,), dtype=jnp.float32)
        wk = jax.random.normal(ks[2], (CQK, C), dtype=jnp.float32) * 0.02
        bk = jnp.zeros((CQK,), dtype=jnp.float32)
        wv = jax.random.normal(ks[3], (C, C), dtype=jnp.float32) * 0.02
        bv = jnp.zeros((C,), dtype=jnp.float32)
        gamma = jnp.ones((1,), dtype=jnp.float32) * 0.5
        return {'x': x, 'wq': wq, 'bq': bq, 'wk': wk, 'bk': bk, 'wv': wv, 'bv': bv, 'gamma': gamma}
    _L0_conv_all = _L0_conv_setup()
    _L0_conv_in = {k: v for k, v in _L0_conv_all.items() if k in ('wq', 'bq', 'wk', 'bk', 'wv', 'bv', 'gamma', )}
    del _L0_conv_all

    return {
        "x": x,
        "L0_conv_wq": _L0_conv_in["wq"],
        "L0_conv_bq": _L0_conv_in["bq"],
        "L0_conv_wk": _L0_conv_in["wk"],
        "L0_conv_bk": _L0_conv_in["bk"],
        "L0_conv_wv": _L0_conv_in["wv"],
        "L0_conv_bv": _L0_conv_in["bv"],
        "L0_conv_gamma": _L0_conv_in["gamma"],
    }

def reference(x, L0_conv_wq, L0_conv_bq, L0_conv_wk, L0_conv_bk, L0_conv_wv, L0_conv_bv, L0_conv_gamma):
    import jax
    import jax.numpy as jnp
    def _L0_conv_ref(x, wq, bq, wk, bk, wv, bv, gamma):
        import jax, jax.numpy as jnp
        import numpy as np
        C = 512
        CQK = C // 8
        q = jnp.einsum('bchw,oc->bohw', x, wq) + bq[None, :, None, None]
        k = jnp.einsum('bchw,oc->bohw', x, wk) + bk[None, :, None, None]
        v = jnp.einsum('bchw,oc->bohw', x, wv) + bv[None, :, None, None]
        att_h = jnp.einsum('bchw,bcgw->bwhg', q, k)
        att_h = jax.nn.softmax(att_h, axis=-1)
        out_h = jnp.einsum('bcgw,bwhg->bchw', v, att_h)
        att_w = jnp.einsum('bchw,bchg->bhwg', q, k)
        att_w = jax.nn.softmax(att_w, axis=-1)
        out_w = jnp.einsum('bchg,bhwg->bchw', v, att_w)
        return gamma[0] * (out_h + out_w) + x

    def _gn(v, G=32, eps=1e-5):
        B_, C_, H_, W_ = v.shape
        g = v.reshape(B_, G, C_ // G, H_, W_)
        m = jnp.mean(g, axis=(2, 3, 4), keepdims=True)
        s = jnp.var(g, axis=(2, 3, 4), keepdims=True)
        return ((g - m) / jnp.sqrt(s + eps)).reshape(v.shape)

    def _ln_c(v, eps=1e-6):
        m = jnp.mean(v, axis=1, keepdims=True)
        s = jnp.var(v, axis=1, keepdims=True)
        return (v - m) / jnp.sqrt(s + eps)

    def _ln_t(v, eps=1e-5):
        m = jnp.mean(v, axis=-1, keepdims=True)
        s = jnp.var(v, axis=-1, keepdims=True)
        return (v - m) / jnp.sqrt(s + eps)

    def _to_tokens(v):
        B_, C_, H_, W_ = v.shape
        return v.reshape(B_, C_, H_ * W_).transpose(0, 2, 1)
    def _from_tokens(t, like):
        B_, C_, H_, W_ = like.shape
        return t.transpose(0, 2, 1).reshape(B_, C_, H_, W_)

    x = _L0_conv_ref(x, L0_conv_wq, L0_conv_bq, L0_conv_wk, L0_conv_bk, L0_conv_wv, L0_conv_bv, L0_conv_gamma)
    return x


_drawn_inputs = setup_inputs


def setup_inputs(seed=0):
    import zlib

    import numpy as np

    out = dict(_drawn_inputs(seed))
    spreads = {'L0_conv_bq': (0.0, 0.299), 'L0_conv_bk': (0.0, 0.8), 'L0_conv_bv': (0.0, 0.1)}
    factors = {}
    for name, (base, spread) in spreads.items():
        noise = np.random.default_rng([zlib.crc32(name.encode()), seed]).standard_normal(out[name].shape)
        drawn = base * np.exp(spread * noise) if base else spread * noise
        out[name] = jnp.asarray(drawn.astype(out[name].dtype))
    for name, factor in factors.items():
        out[name] = (out[name] * factor).astype(out[name].dtype)
    return out
```

```python
from contextlib import ExitStack

import concourse.bass as bass
from concourse import mybir

ALU = mybir.AluOpType
ACT = mybir.ActivationFunctionType
AX_X = mybir.AxisListType.X
F32 = mybir.dt.float32
F32R = mybir.dt.float32r
P = 128


def build(nc, x, wqk_t, bqk, wv_t, bv, gamma, out):
    B, C, H, W = x.shape
    CQK = wqk_t.shape[1] // 2
    KT = C // P
    L = H
    PIX = H * W
    LINES = 2
    UNITS = L // LINES
    ROWS = 4
    GROUPS = H // ROWS
    GP = ROWS * W
    PER_IMAGE = 2 * UNITS
    assert H == W and 2 * CQK == P and C % P == 0 and ROWS == 2 * LINES and GROUPS > 4

    x_rows = x.rearrange("b (k p) h w -> b p k (h w)", p=P)
    out_rows = out.rearrange("b (k p) h w -> b p k (h w)", p=P)

    with ExitStack() as ctx:
        def sb(name, shape, dt=F32):
            return ctx.enter_context(nc.sbuf_tensor(name, shape, dt))

        def ps(name, shape):
            return ctx.enter_context(nc.psum_tensor(name, shape, F32))

        def sem(name):
            return ctx.enter_context(nc.semaphore(name))

        xy = sb("xy", [P, KT, PIX])
        qk = sb("qk", [P, PIX])
        wv_hi = sb("wv_hi", [P, KT, C], F32R)
        wv_lo = sb("wv_lo", [P, KT, C], F32R)
        wqk = sb("wqk", [P, KT, P])
        with nc.sbuf_tensor("x_turned_odd", [L, LINES, C], F32) as x_turned_odd, \
                nc.sbuf_tensor("probs_odd", [L, LINES, L], F32) as probs_odd, \
                nc.sbuf_tensor("probs_turned_odd", [L, LINES, L], F32) as probs_turned_odd:
            pass
        y_hi = sb("y_hi", [P, KT, GP], F32R)
        y_lo = sb("y_lo", [P, KT, GP], F32R)
        x_line = sb("x_line", [P, 2, KT, LINES, L])
        x_turned_even = sb("x_turned_even", [L, LINES, C])
        qk_line = sb("qk_line", [CQK, 2, LINES, L])
        probs_even = sb("probs_even", [L, LINES, L])
        probs_turned_even = sb("probs_turned_even", [L, LINES, L])
        x_turned = [x_turned_even, x_turned_odd]
        probs = [probs_even, probs_odd]
        probs_turned = [probs_turned_even, probs_turned_odd]
        ident = sb("ident", [P, P])
        small = sb("small", [P, 2 + 2 * KT + 3 * 2 * LINES])
        bqk_col = small[:, 0:1]
        gamma_col = small[:, 1:2]
        bv_col = small[:, 2:2 + KT]
        bias_col = small[:, 2 + KT:2 + 2 * KT]
        neg_max, row_sum, row_inv = [
            small[0:L, 2 + 2 * KT + 2 * LINES * n:2 + 2 * KT + 2 * LINES * (n + 1)].rearrange(
                "h (u j) -> h u j", u=2) for n in range(3)]

        xt_ps = [ps("xt_ps0", [P, C]), ps("xt_ps1", [P, C])]
        y_ps = [ps("y_ps0", [P, 512]), ps("y_ps1", [P, 512])]
        score_bank = ps("score_bank", [L, 512])
        pt_bank = ps("pt_bank", [L, 512])
        v_ps = [ps("v_ps0", [P, 512]), ps("v_ps1", [P, 512])]
        qk_ps = v_ps[1][:, 0:GP]
        score_ps = score_bank[:, 0:LINES * L].rearrange("h (j g) -> h j g", j=LINES)
        pt_ps = pt_bank[:, 0:LINES * L].rearrange("g (j h) -> g j h", j=LINES)

        def y_ps_of(j):
            return y_ps[j][:, 0:KT * L].rearrange("p (k g) -> p k g", k=KT)

        weights_in = sem("weights_in")
        x_in = sem("x_in")
        x_line_in = [sem("x_line_in0"), sem("x_line_in1")]
        out_stored = sem("out_stored")
        ident_zero = sem("ident_zero")
        ident_done = sem("ident_done")
        wv_hi_done = sem("wv_hi_done")
        wv_split = sem("wv_split")
        bias_done = sem("bias_done")
        q_staged = sem("q_staged")
        k_staged = sem("k_staged")
        scores_done = sem("scores_done")
        max_done = sem("max_done")
        exp_done = sem("exp_done")
        inv_done = sem("inv_done")
        probs_done = sem("probs_done")
        pt_done = sem("pt_done")
        x_gathered = sem("x_gathered")
        xt_out = [sem("xt_out0"), sem("xt_out1")]
        pt_out = sem("pt_out")
        y_out = [sem("y_out0"), sem("y_out1")]
        xt_done = sem("xt_done")
        mix_done = sem("mix_done")
        y_hi_done = sem("y_hi_done")
        y_lo_done = sem("y_lo_done")
        rest_done = sem("rest_done")
        pool_waited = sem("pool_waited")
        qk_done = sem("qk_done")
        qk_out = sem("qk_out")
        v_done = sem("v_done")
        out_done = sem("out_done")

        wv_raw = xy[:, KT - 1, PIX - KT * C:PIX].rearrange("p (k c) -> p k c", k=KT)
        FIRST_RAW_GROUP = (PIX - KT * C) // GP

        def columns_of(t, first):
            return t.rearrange("p k (h w) -> p k w h", w=W)[:, :, bass.ds(first, LINES), :]

        def column_of(w):
            return xy[:, :, :].rearrange("p k (h w) -> p k h w", w=W)[:, :, :, bass.ds(w, 1)].rearrange(
                "p k h o -> p k (h o)")

        def row_pixels(row, n):
            return bass.ds(row * W, n * W)

        def qk_lines(part, rows, i):
            if rows:
                return qk[part, row_pixels(i * LINES, LINES)].rearrange("p (j g) -> p j g", j=LINES)
            return qk[part, :].rearrange("p (h w) -> p w h", w=W)[:, bass.ds(i * LINES, LINES), :]

        def run(eng, first_image, start_columns, column_unit, start_rows, row_group, tail):
            def image(b, is_last):
                start_columns(b)
                with eng.Fori(0, UNITS // 2 - 1) as i:
                    for par in range(2):
                        column_unit(b, i * 2 + par, par, True)
                for par in range(2):
                    column_unit(b, UNITS - 2 + par, par, False)
                start_rows(b)
                first = 0
                if not is_last:
                    row_group(b, 0, True, False, False)
                    row_group(b, 1, True, False, True)
                    first = 2
                with eng.Fori(first, GROUPS - 1) as g:
                    row_group(b, g, True, not is_last, not is_last)
                row_group(b, GROUPS - 1, False, not is_last, not is_last)
                if not is_last:
                    tail(b)

            first_image()
            with eng.Fori(0, B - 1) as b:
                image(b, False)
            image(B - 1, True)

        def past(n):
            return n + 1

        def start_at_one(eng, *semaphores):
            for semaphore in semaphores:
                eng.sem_inc(semaphore, 1)

        def unit_of_columns(b, i):
            return b * PER_IMAGE + i

        def unit_of_rows(b, i):
            return b * PER_IMAGE + i + UNITS

        block = ctx.enter_context(nc.Block())

        @block.sync
        def _(sp):
            def load_group(b, g, count):
                sp.wait_ge(x_in, past(count * 16))
                sp.dma_start(xy[:, :, row_pixels(g * ROWS, ROWS)],
                             x_rows[b, :, :, row_pixels(g * ROWS, ROWS)]).then_inc(x_in, 16)

            def load_lines(b, i, par):
                sp.dma_start(x_line[:, par, :, :, :].rearrange("p k j g -> p k (j g)"),
                             x_rows[b, :, :, row_pixels(i * LINES, LINES)]).then_inc(x_line_in[par], 16)

            def first_image():
                start_at_one(sp, x_in, *x_line_in, out_stored)
                sp.dma_start(wv_raw, wv_t.rearrange("(k p) c -> p k c", p=P)).then_inc(weights_in, 16)
                sp.dma_start(wqk[:, :, :], wqk_t.rearrange("(k p) c -> p k c", p=P)).then_inc(weights_in, 16)
                sp.dma_start(bqk_col, bqk).then_inc(weights_in, 16)
                sp.dma_start(bv_col, bv).then_inc(weights_in, 16)
                sp.dma_start(gamma_col, gamma.to_broadcast([P, 1])).then_inc(weights_in, 16)
                with sp.Fori(0, FIRST_RAW_GROUP) as g:
                    load_group(0, g, g)
                sp.wait_ge(wv_split, 1)
                with sp.Fori(FIRST_RAW_GROUP, GROUPS) as g:
                    load_group(0, g, g)

            def start_columns(b):
                pass

            def column_unit(b, i, par, more):
                if not more:
                    sp.wait_ge(xt_done, past((unit_of_columns(b, i) + 1) * LINES))
                    load_lines(b, par, par)

            def start_rows(b):
                pass

            def row_group(b, g, more, project, feed):
                group = b * GROUPS + g
                if feed:
                    sp.wait_ge(out_stored, past(group * (16 * KT)))
                    load_group(b + 1, g - 1, group + (GROUPS - 1))
                if more:
                    for par in range(2):
                        sp.wait_ge(rest_done, past(group * 2 + 1 + par))
                        load_lines(b, g * 2 + 2 + par, par)
                for m in range(KT):
                    sp.wait_ge(out_done, past(group * KT + m + 1))
                    sp.dma_start(out_rows[b, :, m, row_pixels(g * ROWS, ROWS)],
                                 xy[:, m, row_pixels(g * ROWS, ROWS)]).then_inc(out_stored, 16)

            def tail(b):
                group = b * GROUPS + GROUPS
                sp.wait_ge(out_stored, past(group * (16 * KT)))
                load_group(b + 1, GROUPS - 1, group + (GROUPS - 1))

            run(sp, first_image, start_columns, column_unit, start_rows, row_group, tail)
            sp.wait_ge(out_stored, past(16 * KT * B * GROUPS))

        @block.tensor
        def _(pe):
            def make_qk(g, count):
                pe.wait_ge(x_in, past(count * 16 + 16))
                pe.wait_ge(qk_out, past(count))
                for k in range(KT):
                    mm = pe.matmul(qk_ps, wqk[:, k, :], xy[:, k, row_pixels(g * ROWS, ROWS)],
                                   start=(k == 0), stop=(k == KT - 1))
                mm.then_inc(qk_done, 1)

            def scores(u):
                pe.wait_ge(exp_done, past(u))
                pe.wait_ge(q_staged, past(u + 1))
                pe.wait_ge(k_staged, past(u + 1))
                for j in range(LINES):
                    mm = pe.matmul(score_ps[:, j, :], qk_line[:, 0, j, :], qk_line[:, 1, j, :],
                                   start=True, stop=True)
                mm.then_inc(scores_done, 1)

            def turn_x(u, par):
                for j in range(LINES):
                    pe.wait_ge(xt_out[j], past(u))
                    for k in range(KT):
                        mm = pe.transpose(xt_ps[j][0:L, k * P:(k + 1) * P], x_line[:, par, k, j, :], ident[:, :])
                    mm.then_inc(xt_done, 1)

            def turn_column_x(b, i, par):
                pe.wait_ge(x_gathered, past(b * UNITS + i + 1))
                turn_x(unit_of_columns(b, i), par)

            def turn_row_x(b, i, par):
                pe.wait_ge(x_line_in[par], past((b * UNITS + i - par) * 8 + 16))
                turn_x(unit_of_rows(b, i), par)

            def turn_probs(u, buf):
                pe.wait_ge(probs_done, past(u + 1))
                pe.wait_ge(pt_out, past(u))
                for j in range(LINES):
                    mm = pe.transpose(pt_ps[:, j, :], probs[buf][:, j, :], ident[0:L, 0:L])
                mm.then_inc(pt_done, 1)

            def mix(u, j, buf):
                pe.wait_ge(pt_out, past(u + 1))
                pe.wait_ge(xt_out[j], past(u + 1))
                pe.wait_ge(y_out[j], past(u))
                for k in range(KT):
                    mm = pe.matmul(y_ps_of(j)[:, k, :], x_turned[buf][:, j, k * P:(k + 1) * P],
                                   probs_turned[buf][:, j, :], start=True, stop=True)
                mm.then_inc(mix_done, 1)

            def values(group, m):
                if m >= 2:
                    pe.wait_ge(out_done, past(group * KT + (m - 1)))
                for n, (w, y) in enumerate([(wv_hi, y_hi), (wv_lo, y_hi), (wv_hi, y_lo)]):
                    if m == 0 and n == 0:
                        pe.wait_ge(y_hi_done, past(group * 2 + 2))
                    if m == 0 and n == 2:
                        pe.wait_ge(y_lo_done, past(group * 2 + 2))
                    for k in range(KT):
                        mm = pe.matmul(v_ps[m % 2][:, 0:GP], w[:, k, m * P:(m + 1) * P], y[:, k, :],
                                       start=(n == 0 and k == 0), stop=(n == 2 and k == KT - 1))
                mm.then_inc(v_done, 1)

            def first_image():
                start_at_one(pe, scores_done, xt_done, pt_done, mix_done, qk_done, v_done)
                pe.wait_ge(ident_done, 1)
                pe.wait_ge(weights_in, 16 * 5)
                pe.wait_ge(wv_split, 1)
                with pe.Fori(0, GROUPS) as g:
                    make_qk(g, g)

            def start_columns(b):
                u = unit_of_columns(b, 0)
                scores(u)
                turn_column_x(b, 0, 0)
                turn_probs(u, 0)
                scores(u + 1)
                turn_column_x(b, 1, 1)

            def column_unit(b, i, par, more):
                u = unit_of_columns(b, i)
                mix(u, 0, par)
                if more:
                    scores(u + 2)
                if more or par == 0:
                    turn_probs(u + 1, 1 - par)
                mix(u, 1, par)
                if more:
                    turn_column_x(b, i + 2, par)

            def start_rows(b):
                u = unit_of_rows(b, 0)
                for par in range(2):
                    scores(u + par)
                    turn_row_x(b, par, par)
                    turn_probs(u + par, 0)
                    for j in range(LINES):
                        mix(u + par, j, 0)

            def row_group(b, g, more, project, feed):
                group = b * GROUPS + g
                u = unit_of_rows(b, g * 2)
                pe.wait_ge(out_done, past(group * KT))
                if project:
                    make_qk(g - 2, group + (GROUPS - 2))
                values(group, 0)
                if more:
                    scores(u + 2)
                if project:
                    pe.wait_ge(qk_out, past(group + (GROUPS - 1)))
                values(group, 1)
                if more:
                    turn_row_x(b, g * 2 + 2, 0)
                    turn_probs(u + 2, 0)
                    scores(u + 3)
                values(group, 2)
                if more:
                    mix(u + 2, 0, 0)
                    turn_row_x(b, g * 2 + 3, 1)
                    mix(u + 2, 1, 0)
                    turn_probs(u + 3, 0)
                values(group, 3)
                if more:
                    mix(u + 3, 0, 0)
                    mix(u + 3, 1, 0)

            def tail(b):
                pe.wait_ge(out_done, past(b * (GROUPS * KT) + GROUPS * KT))
                for g in (GROUPS - 2, GROUPS - 1):
                    make_qk(g, b * GROUPS + (GROUPS + g))

            run(pe, first_image, start_columns, column_unit, start_rows, row_group, tail)

        @block.scalar
        def _(act):
            def take_qk(g, count):
                act.wait_ge(qk_done, past(count + 1))
                act.activation(qk[:, row_pixels(g * ROWS, ROWS)], qk_ps, ACT.Identity,
                               bias=bqk_col).then_inc(qk_out, 1)

            def take_turned_x(u, buf, mixed):
                act.wait_ge(mix_done, past(mixed))
                act.wait_ge(xt_done, past(u * 2 + 1))
                act.copy(x_turned[buf][:, 0, :], xt_ps[0][0:L, 0:C]).then_inc(xt_out[0], 1)

            def take_turned_probs(u, buf, mixed):
                act.wait_ge(mix_done, past(mixed))
                act.wait_ge(pt_done, past(u + 1))
                act.copy(probs_turned[buf][:, :, :], pt_ps).then_inc(pt_out, 1)

            def take_column(i, u):
                act.wait_ge(mix_done, past(u * 2 + 1))
                act.copy(column_of(i * LINES), y_ps_of(0)).then_inc(y_out[0], 1)

            def exps(u, par, buf, turned):
                act.wait_ge(pt_done, past(turned))
                act.wait_ge(max_done, past(u + 1))
                for j in range(LINES):
                    e = act.activation(probs[buf][:, j, :], score_ps[:, j, :], ACT.Exp,
                                       bias=neg_max[:, par, j:j + 1], accum_out=row_sum[:, par, j:j + 1])
                e.then_inc(exp_done, 1)

            def take_y_hi(g, u, group, half):
                act.wait_ge(y_out[1], past(u + 1))
                if half == 0:
                    act.wait_ge(v_done, past(group * KT))
                act.copy(y_hi[:, :, half * LINES * W:(half + 1) * LINES * W],
                         xy[:, :, row_pixels(g * ROWS + half * LINES, LINES)]).then_inc(y_hi_done, 1)

            def first_image():
                start_at_one(act, exp_done, pt_out, xt_out[0], y_out[0], y_hi_done, qk_out)
                act.wait_ge(weights_in, 16 * 5)
                act.copy(wv_hi[:, :, :], wv_raw).then_inc(wv_hi_done, 1)
                with act.Fori(0, GROUPS) as g:
                    take_qk(g, g)

            def start_columns(b):
                u = unit_of_columns(b, 0)
                exps(u, 0, 0, u)
                take_turned_x(u, 0, u * 2)
                take_turned_probs(u, 0, u * 2)
                exps(u + 1, 1, 1, u)
                take_turned_x(u + 1, 1, u * 2)

            def column_unit(b, i, par, more):
                u = unit_of_columns(b, i)
                if more or par == 0:
                    take_turned_probs(u + 1, 1 - par, u * 2)
                take_column(i, u)
                if more:
                    exps(u + 2, par, par, u + 1)
                    take_turned_x(u + 2, par, u * 2 + 1)

            def start_rows(b):
                u = unit_of_rows(b, 0)
                for par in range(2):
                    exps(u + par, par, 0, u + par)
                    take_turned_x(u + par, 0, u * 2 + par * 2)
                    take_turned_probs(u + par, 0, u * 2 + par * 2)

            def row_group(b, g, more, project, feed):
                group = b * GROUPS + g
                u = unit_of_rows(b, g * 2)
                take_y_hi(g, u, group, 0)
                take_y_hi(g, u + 1, group, 1)
                if project:
                    take_qk(g - 2, group + (GROUPS - 2))
                if more:
                    exps(u + 2, 0, 0, u + 2)
                    take_turned_x(u + 2, 0, u * 2 + 3)
                    take_turned_probs(u + 2, 0, u * 2 + 4)
                    exps(u + 3, 1, 0, u + 3)
                    take_turned_x(u + 3, 0, u * 2 + 5)
                    take_turned_probs(u + 3, 0, u * 2 + 6)

            def tail(b):
                for g in (GROUPS - 2, GROUPS - 1):
                    take_qk(g, b * GROUPS + (GROUPS + g))

            run(act, first_image, start_columns, column_unit, start_rows, row_group, tail)

        @block.vector
        def _(dve):
            def stage_k(i, u, rows):
                dve.wait_ge(scores_done, past(u))
                dve.tensor_copy(qk_line[:, 1, :, :], qk_lines(slice(CQK, P), rows, i)).then_inc(k_staged, 1)

            def stage_row_q(i):
                dve.tensor_copy(qk_line[:, 0, :, :], qk_lines(slice(0, CQK), True, i)).then_inc(q_staged, 1)

            def gather(i, par, turned):
                dve.wait_ge(xt_done, past(turned))
                dve.tensor_copy(x_line[:, par, :, :, :], columns_of(xy[:, :, :], i * LINES))\
                   .then_inc(x_gathered, 1)

            def row_max(u, par):
                dve.wait_ge(scores_done, past(u + 1))
                dve.tensor_reduce(neg_max[:, par, :], score_ps, AX_X, ALU.max, negate=True)\
                   .then_inc(max_done, 1)

            def divide(u, par, buf):
                dve.wait_ge(exp_done, past(u + 1))
                dve.reciprocal(row_inv[:, par, :], row_sum[:, par, :]).then_inc(inv_done, 1)
                dve.wait_ge(inv_done, past(u + 1))
                for j in range(LINES):
                    d = dve.tensor_scalar(probs[buf][:, j, :], probs[buf][:, j, :], row_inv[:, par, j:j + 1],
                                          None, ALU.mult)
                d.then_inc(probs_done, 1)

            def take_turned_x(u, buf, mixed):
                dve.wait_ge(mix_done, past(mixed))
                dve.wait_ge(xt_done, past(u * 2 + 2))
                dve.tensor_copy(x_turned[buf][:, 1, :], xt_ps[1][0:L, 0:C]).then_inc(xt_out[1], 1)

            def take_column(i, u):
                dve.wait_ge(mix_done, past(u * 2 + 2))
                dve.tensor_copy(column_of(i * LINES + 1), y_ps_of(1)).then_inc(y_out[1], 1)

            def add_row(i, u, j):
                row = xy[:, :, row_pixels(i * LINES + j, 1)]
                dve.wait_ge(mix_done, past(u * 2 + (j + 1)))
                dve.tensor_tensor(row, y_ps_of(j), row, ALU.add).then_inc(y_out[j], 1)

            def take_y_lo(g, group, half):
                dve.wait_ge(y_hi_done, past(group * 2 + (half + 1)))
                part = slice(half * LINES * W, (half + 1) * LINES * W)
                dve.tensor_tensor(y_lo[:, :, part], xy[:, :, row_pixels(g * ROWS + half * LINES, LINES)],
                                  y_hi[:, :, part].bitcast(F32), ALU.subtract).then_inc(y_lo_done, 1)

            def take_output(g, group, m):
                if m == 0:
                    dve.wait_ge(rest_done, past(group * 2 + 2))
                dve.wait_ge(v_done, past(group * KT + (m + 1)))
                rest = xy[:, m, row_pixels(g * ROWS, ROWS)]
                dve.scalar_tensor_tensor(out=rest, in0=v_ps[m % 2][:, 0:GP], scalar=gamma_col, in1=rest,
                                         op0=ALU.mult, op1=ALU.add).then_inc(out_done, 1)

            def first_image():
                start_at_one(dve, k_staged, x_gathered, max_done, inv_done, probs_done, xt_out[1], y_out[1],
                             y_lo_done, out_done)
                dve.wait_ge(weights_in, 16 * 5)
                dve.tensor_scalar(bias_col, bv_col, gamma_col, 2.0, ALU.mult, ALU.mult).then_inc(bias_done, 1)
                dve.wait_ge(wv_hi_done, 1)
                dve.tensor_tensor(wv_lo[:, :, :], wv_raw, wv_hi[:, :, :].bitcast(F32), ALU.subtract)\
                   .then_inc(wv_split, 1)

            def start_columns(b):
                u = unit_of_columns(b, 0)
                dve.wait_ge(qk_out, past(b * GROUPS + GROUPS))
                for par in range(2):
                    stage_k(par, u + par, False)
                    gather(par, par, u * 2)
                    row_max(u + par, par)
                    divide(u + par, par, par)
                    take_turned_x(u + par, par, u * 2)

            def column_unit(b, i, par, more):
                u = unit_of_columns(b, i)
                if more:
                    stage_k(i + 2, u + 2, False)
                    gather(i + 2, par, u * 2 + 2)
                    row_max(u + 2, par)
                take_column(i, u)
                if more:
                    divide(u + 2, par, par)
                    take_turned_x(u + 2, par, u * 2 + 2)

            def start_rows(b):
                u = unit_of_rows(b, 0)
                dve.wait_ge(y_out[1], past(u))
                for par in range(2):
                    stage_k(par, u + par, True)
                    stage_row_q(par)
                    row_max(u + par, par)
                    divide(u + par, par, 0)
                    take_turned_x(u + par, 0, u * 2 + par * 2)
                    for j in range(LINES):
                        add_row(par, u + par, j)

            def row_group(b, g, more, project, feed):
                group = b * GROUPS + g
                i = g * 2
                u = unit_of_rows(b, i)
                take_y_lo(g, group, 0)
                take_y_lo(g, group, 1)
                if more:
                    stage_k(i + 2, u + 2, True)
                    stage_row_q(i + 2)
                take_output(g, group, 0)
                if more:
                    row_max(u + 2, 0)
                    stage_k(i + 3, u + 3, True)
                    stage_row_q(i + 3)
                    divide(u + 2, 0, 0)
                take_output(g, group, 1)
                if more:
                    take_turned_x(u + 2, 0, u * 2 + 4)
                    row_max(u + 3, 1)
                    divide(u + 3, 1, 0)
                take_output(g, group, 2)
                if more:
                    add_row(i + 2, u + 2, 0)
                    take_turned_x(u + 3, 0, u * 2 + 6)
                    add_row(i + 2, u + 2, 1)
                take_output(g, group, 3)
                if more:
                    add_row(i + 3, u + 3, 0)
                    add_row(i + 3, u + 3, 1)

            def tail(b):
                pass

            run(dve, first_image, start_columns, column_unit, start_rows, row_group, tail)

        @block.gpsimd
        def _(pool):
            def wait_alone(semaphore, value):
                pool.wait_ge(semaphore, value).then_inc(pool_waited, 1)

            def stage_column_q(i, u):
                wait_alone(scores_done, past(u))
                pool.tensor_copy(qk_line[:, 0, :, :], qk_lines(slice(0, CQK), False, i)).then_inc(q_staged, 1)

            def rest(g, group, half):
                wait_alone(y_lo_done, past(group * 2 + (half + 1)))
                pool.tensor_tensor(xy[:, :, row_pixels(g * ROWS + half * LINES, LINES)],
                                   x_line[:, half, :, :, :].rearrange("p k j g -> p k (j g)"),
                                   bias_col.rearrange("p (k o) -> p k o", o=1)
                                   .to_broadcast([P, KT, LINES * W]), ALU.add).then_inc(rest_done, 1)

            def first_image():
                start_at_one(pool, q_staged, rest_done)
                pool.memset(ident[:, :], 0.0).then_inc(ident_zero, 1)
                pool.wait_ge(ident_zero, 1)
                pool.affine_select(out=ident[:, :], in_=ident[:, :], compare_op=ALU.not_equal, fill=1.0,
                                   base=0, pattern=[[-1, P]], channel_multiplier=1).then_inc(ident_done, 1)
                pool.wait_ge(bias_done, 1)

            def start_columns(b):
                u = unit_of_columns(b, 0)
                wait_alone(qk_out, past(b * GROUPS + GROUPS))
                for par in range(2):
                    stage_column_q(par, u + par)

            def column_unit(b, i, par, more):
                if more:
                    stage_column_q(i + 2, unit_of_columns(b, i + 2))

            def start_rows(b):
                pass

            def row_group(b, g, more, project, feed):
                for half in range(2):
                    rest(g, b * GROUPS + g, half)

            def tail(b):
                pass

            run(pool, first_image, start_columns, column_unit, start_rows, row_group, tail)


def kernel(x, L0_conv_wq, L0_conv_bq, L0_conv_wk, L0_conv_bk, L0_conv_wv, L0_conv_bv, L0_conv_gamma):
    import numpy as np
    import concourse.bacc as bacc
    from concourse.bass_utils import run_bass_kernel_spmd

    x = np.ascontiguousarray(x)
    C = x.shape[1]
    arrays = {
        "x": x,
        "wqk_t": np.ascontiguousarray(np.concatenate([L0_conv_wq, L0_conv_wk]).T),
        "bqk": np.concatenate([L0_conv_bq, L0_conv_bk]).reshape(P, 1),
        "wv_t": np.ascontiguousarray(np.asarray(L0_conv_wv).T),
        "bv": np.ascontiguousarray(np.asarray(L0_conv_bv).reshape(C // P, P).T),
        "gamma": np.asarray(L0_conv_gamma).reshape(1, 1),
    }
    nc = bacc.Bacc("TRN2", target_bir_lowering=False, num_devices=1, dynamic_dma_scratch_size=64)
    args = [nc.dram_tensor(n, a.shape, mybir.dt.from_np(a.dtype), kind="ExternalInput").ap()
            for n, a in arrays.items()]
    out = nc.dram_tensor("out", x.shape, F32, kind="ExternalOutput").ap()
    build(nc, *args, out)
    r = run_bass_kernel_spmd(nc, [arrays], core_ids=[0])
    return r.results[0]["out"]
```

```python
from contextlib import ExitStack

import concourse.bass as bass
from concourse import mybir

ALU = mybir.AluOpType
ACT = mybir.ActivationFunctionType
AX_X = mybir.AxisListType.X
F32 = mybir.dt.float32
F32R = mybir.dt.float32r
P = 128


def build(nc, x, wqk_t, bqk, wv_t, bv, gamma, out):
    B, C, H, W = x.shape
    CQK = wqk_t.shape[1] // 2
    KT = C // P
    L = H
    PIX = H * W
    LINES = 2
    UNITS = L // LINES
    ROWS = 4
    GROUPS = H // ROWS
    GP = ROWS * W
    PER_IMAGE = 2 * UNITS
    assert H == W and 2 * CQK == P and C % P == 0 and ROWS == 2 * LINES and GROUPS > 4

    x_rows = x.rearrange("b (k p) h w -> b p k (h w)", p=P)
    out_rows = out.rearrange("b (k p) h w -> b p k (h w)", p=P)

    with ExitStack() as ctx:
        def sb(name, shape, dt=F32):
            return ctx.enter_context(nc.sbuf_tensor(name, shape, dt))

        def ps(name, shape):
            return ctx.enter_context(nc.psum_tensor(name, shape, F32))

        def sem(name):
            return ctx.enter_context(nc.semaphore(name))

        xy = sb("xy", [P, KT, PIX])
        qk = sb("qk", [P, PIX])
        wv_hi = sb("wv_hi", [P, KT, C], F32R)
        wv_lo = sb("wv_lo", [P, KT, C], F32R)
        wqk = sb("wqk", [P, KT, P])
        with nc.sbuf_tensor("x_turned_odd", [L, LINES, C], F32) as x_turned_odd, \
                nc.sbuf_tensor("probs_odd", [L, LINES, L], F32) as probs_odd, \
                nc.sbuf_tensor("probs_turned_odd", [L, LINES, L], F32) as probs_turned_odd:
            pass
        y_hi = sb("y_hi", [P, KT, GP], F32R)
        y_lo = sb("y_lo", [P, KT, GP], F32R)
        x_line = sb("x_line", [P, 2, KT, LINES, L])
        x_turned_even = sb("x_turned_even", [L, LINES, C])
        qk_line = sb("qk_line", [CQK, 2, LINES, L])
        probs_even = sb("probs_even", [L, LINES, L])
        probs_turned_even = sb("probs_turned_even", [L, LINES, L])
        x_turned = [x_turned_even, x_turned_odd]
        probs = [probs_even, probs_odd]
        probs_turned = [probs_turned_even, probs_turned_odd]
        ident = sb("ident", [P, P])
        small = sb("small", [P, 2 + 2 * KT + 3 * 2 * LINES])
        bqk_col = small[:, 0:1]
        gamma_col = small[:, 1:2]
        bv_col = small[:, 2:2 + KT]
        bias_col = small[:, 2 + KT:2 + 2 * KT]
        neg_max, row_sum, row_inv = [
            small[0:L, 2 + 2 * KT + 2 * LINES * n:2 + 2 * KT + 2 * LINES * (n + 1)].rearrange(
                "h (u j) -> h u j", u=2) for n in range(3)]

        xt_ps = [ps("xt_ps0", [P, C]), ps("xt_ps1", [P, C])]
        y_ps = [ps("y_ps0", [P, 512]), ps("y_ps1", [P, 512])]
        score_bank = ps("score_bank", [L, 512])
        pt_bank = ps("pt_bank", [L, 512])
        v_ps = [ps("v_ps0", [P, 512]), ps("v_ps1", [P, 512])]
        qk_ps = v_ps[1][:, 0:GP]
        qk_alone_ps = [y[:, 0:GP] for y in y_ps]
        score_ps = score_bank[:, 0:LINES * L].rearrange("h (j g) -> h j g", j=LINES)
        pt_ps = pt_bank[:, 0:LINES * L].rearrange("g (j h) -> g j h", j=LINES)

        def y_ps_of(j):
            return y_ps[j][:, 0:KT * L].rearrange("p (k g) -> p k g", k=KT)

        small_in = sem("small_in")
        wv_in = sem("wv_in")
        x_first_in = [sem("x_first_in0"), sem("x_first_in1")]
        x_in = sem("x_in")
        x_line_in = [sem("x_line_in0"), sem("x_line_in1")]
        out_stored = sem("out_stored")
        ident_zero = sem("ident_zero")
        ident_done = sem("ident_done")
        wv_hi_done = sem("wv_hi_done")
        wv_split = sem("wv_split")
        bias_done = sem("bias_done")
        q_staged = sem("q_staged")
        k_staged = sem("k_staged")
        scores_done = sem("scores_done")
        max_done = sem("max_done")
        exp_done = sem("exp_done")
        inv_done = sem("inv_done")
        probs_done = sem("probs_done")
        pt_done = sem("pt_done")
        x_gathered = sem("x_gathered")
        xt_out = [sem("xt_out0"), sem("xt_out1")]
        pt_out = sem("pt_out")
        y_out = [sem("y_out0"), sem("y_out1")]
        xt_done = sem("xt_done")
        mix_done = sem("mix_done")
        y_hi_done = [sem("y_hi_done0"), sem("y_hi_done2"), sem("y_hi_done3")]
        y_lo_done = [sem("y_lo_done0"), sem("y_lo_done2")]
        rest_done = sem("rest_done")
        pool_waited = sem("pool_waited")
        qk_done = sem("qk_done")
        qk_out = sem("qk_out")
        x_whole = sem("x_whole")
        v_done = sem("v_done")
        out_done = sem("out_done")

        wv_raw = xy[:, KT - 1, PIX - KT * C:PIX].rearrange("p (k c) -> p k c", k=KT)
        FIRST_RAW_PAIR = (PIX - KT * C) // (2 * GP)
        LINE_LOADS = GROUPS + 1
        FEEDS = GROUPS - 1

        def columns_of(t, first):
            return t.rearrange("p k (h w) -> p k w h", w=W)[:, :, bass.ds(first, LINES), :]

        def column_of(w):
            return xy[:, :, :].rearrange("p k (h w) -> p k h w", w=W)[:, :, :, bass.ds(w, 1)].rearrange(
                "p k h o -> p k (h o)")

        def row_pixels(row, n):
            return bass.ds(row * W, n * W)

        def qk_lines(part, rows, i):
            if rows:
                return qk[part, row_pixels(i * LINES, LINES)].rearrange("p (j g) -> p j g", j=LINES)
            return qk[part, :].rearrange("p (h w) -> p w h", w=W)[:, bass.ds(i * LINES, LINES), :]

        def run(eng, first_image, start_columns, column_unit, start_rows, row_group, tail):
            def image(b, is_last):
                start_columns(b)
                with eng.Fori(0, UNITS // 2 - 2) as i:
                    for par in range(2):
                        column_unit(b, i * 2 + par, par, UNITS)
                for n in range(4, 0, -1):
                    column_unit(b, UNITS - n, n % 2, n)
                start_rows(b)
                first = 0
                if not is_last:
                    row_group(b, 0, True, False, False)
                    row_group(b, 1, True, False, True)
                    first = 2
                with eng.Fori(first, GROUPS - 1) as g:
                    row_group(b, g, True, not is_last, not is_last)
                row_group(b, GROUPS - 1, False, not is_last, not is_last)
                if not is_last:
                    tail(b)

            first_image()
            with eng.Fori(0, B - 1) as b:
                image(b, False)
            image(B - 1, True)

        def past(n):
            return n + 1

        def start_at_one(eng, *semaphores):
            for semaphore in semaphores:
                eng.sem_inc(semaphore, 1)

        def unit_of_columns(b, i):
            return b * PER_IMAGE + i

        def unit_of_rows(b, i):
            return b * PER_IMAGE + i + UNITS

        block = ctx.enter_context(nc.Block())

        @block.sync
        def _(sp):
            def load_first_pair(pair):
                for par in range(2):
                    sp.wait_ge(x_first_in[par], past(pair * 16))
                    rows = row_pixels((pair * 2 + par) * ROWS, ROWS)
                    sp.dma_start(xy[:, :, rows], x_rows[0, :, :, rows]).then_inc(x_first_in[par], 16)

            def load_group(b, g):
                sp.wait_ge(x_in, past(((b - 1) * FEEDS + g) * 16))
                sp.dma_start(xy[:, :, row_pixels(g * ROWS, ROWS)],
                             x_rows[b, :, :, row_pixels(g * ROWS, ROWS)]).then_inc(x_in, 16)

            def load_lines(b, i, par):
                sp.dma_start(x_line[:, par, :, :, :].rearrange("p k j g -> p k (j g)"),
                             x_rows[b, :, :, row_pixels(i * LINES, LINES)]).then_inc(x_line_in[par], 16)

            def first_image():
                start_at_one(sp, *x_first_in, x_in, *x_line_in, out_stored)
                sp.dma_start(wqk[:, :, :], wqk_t.rearrange("(k p) c -> p k c", p=P)).then_inc(small_in, 16)
                sp.dma_start(bqk_col, bqk).then_inc(small_in, 16)
                sp.dma_start(bv_col, bv).then_inc(small_in, 16)
                sp.dma_start(gamma_col, gamma.to_broadcast([P, 1])).then_inc(small_in, 16)
                load_first_pair(0)
                sp.dma_start(wv_raw, wv_t.rearrange("(k p) c -> p k c", p=P)).then_inc(wv_in, 16)
                with sp.Fori(1, FIRST_RAW_PAIR) as pair:
                    load_first_pair(pair)
                sp.wait_ge(wv_split, 1)
                with sp.Fori(FIRST_RAW_PAIR, GROUPS // 2) as pair:
                    load_first_pair(pair)

            def start_columns(b):
                pass

            def column_unit(b, i, par, left):
                if left <= 2:
                    sp.wait_ge(xt_done, past((unit_of_columns(b, i) + 1) * LINES))
                    load_lines(b, par, par)

            def start_rows(b):
                pass

            def row_group(b, g, more, project, feed):
                group = b * GROUPS + g
                if more or feed:
                    for par in range(2):
                        sp.wait_ge(rest_done, past(group * 2 + 1 + par))
                        if more:
                            load_lines(b, g * 2 + 2 + par, par)
                        else:
                            load_lines(b + 1, UNITS - 2 + par, par)
                if feed:
                    sp.wait_ge(out_stored, past(group * (16 * KT)))
                    load_group(b + 1, g - 1)
                for m in range(KT):
                    sp.wait_ge(out_done, past(group * KT + m + 1))
                    sp.dma_start(out_rows[b, :, m, row_pixels(g * ROWS, ROWS)],
                                 xy[:, m, row_pixels(g * ROWS, ROWS)]).then_inc(out_stored, 16)

            def tail(b):
                pass

            run(sp, first_image, start_columns, column_unit, start_rows, row_group, tail)
            sp.wait_ge(out_stored, past(16 * KT * B * GROUPS))

        @block.tensor
        def _(pe):
            def make_qk(g, into):
                for k in range(KT):
                    mm = pe.matmul(into, wqk[:, k, :], xy[:, k, row_pixels(g * ROWS, ROWS)],
                                   start=(k == 0), stop=(k == KT - 1))
                mm.then_inc(qk_done, 1)

            def make_first_qk(pair, again):
                for par in range(2):
                    pe.wait_ge(x_first_in[par], past(pair * 16 + 16))
                    if again:
                        pe.wait_ge(qk_out, past(pair * 2 + par - 1))
                    make_qk(pair * 2 + par, qk_alone_ps[par])

            def scores(u):
                pe.wait_ge(exp_done, past(u))
                pe.wait_ge(q_staged, past(u + 1))
                pe.wait_ge(k_staged, past(u + 1))
                for j in range(LINES):
                    mm = pe.matmul(score_ps[:, j, :], qk_line[:, 0, j, :], qk_line[:, 1, j, :],
                                   start=True, stop=True)
                mm.then_inc(scores_done, 1)

            def turn_x(u, par):
                for j in range(LINES):
                    pe.wait_ge(xt_out[j], past(u))
                    for k in range(KT):
                        mm = pe.transpose(xt_ps[j][0:L, k * P:(k + 1) * P], x_line[:, par, k, j, :], ident[:, :])
                    mm.then_inc(xt_done, 1)

            def turn_column_x(b, i, par):
                pe.wait_ge(x_gathered, past(b * UNITS + i + 1))
                turn_x(unit_of_columns(b, i), par)

            def turn_row_x(b, i, par):
                pe.wait_ge(x_line_in[par], past(b * (LINE_LOADS * 16) + (i - par) * 8 + 16))
                turn_x(unit_of_rows(b, i), par)

            def turn_probs(u, buf):
                pe.wait_ge(probs_done, past(u + 1))
                pe.wait_ge(pt_out, past(u))
                for j in range(LINES):
                    mm = pe.transpose(pt_ps[:, j, :], probs[buf][:, j, :], ident[0:L, 0:L])
                mm.then_inc(pt_done, 1)

            def mix(u, j, buf):
                pe.wait_ge(pt_out, past(u + 1))
                pe.wait_ge(xt_out[j], past(u + 1))
                pe.wait_ge(y_out[j], past(u))
                for k in range(KT):
                    mm = pe.matmul(y_ps_of(j)[:, k, :], x_turned[buf][:, j, k * P:(k + 1) * P],
                                   probs_turned[buf][:, j, :], start=True, stop=True)
                mm.then_inc(mix_done, 1)

            def values(group, m):
                if m >= 2:
                    pe.wait_ge(out_done, past(group * KT + (m - 1)))
                for n, (w, y) in enumerate([(wv_hi, y_hi), (wv_lo, y_hi), (wv_hi, y_lo)]):
                    if m == 0 and n == 0:
                        for done in y_hi_done:
                            pe.wait_ge(done, past(group + 1))
                    if m == 0 and n == 2:
                        for done in y_lo_done:
                            pe.wait_ge(done, past(group + 1))
                    for k in range(KT):
                        mm = pe.matmul(v_ps[m % 2][:, 0:GP], w[:, k, m * P:(m + 1) * P], y[:, k, :],
                                       start=(n == 0 and k == 0), stop=(n == 2 and k == KT - 1))
                mm.then_inc(v_done, 1)

            def first_image():
                start_at_one(pe, scores_done, xt_done, pt_done, mix_done, qk_done, v_done)
                pe.wait_ge(ident_done, 1)
                pe.wait_ge(small_in, 16 * 4)
                make_first_qk(0, False)
                with pe.Fori(1, GROUPS // 2) as pair:
                    make_first_qk(pair, True)
                pe.wait_ge(wv_split, 1)

            def start_columns(b):
                u = unit_of_columns(b, 0)
                scores(u)
                turn_column_x(b, 0, 0)
                turn_probs(u, 0)
                scores(u + 1)
                turn_column_x(b, 1, 1)

            def column_unit(b, i, par, left):
                u = unit_of_columns(b, i)
                mix(u, 0, par)
                scores(u + 2)
                turn_probs(u + 1, 1 - par)
                mix(u, 1, par)
                if left > 2:
                    turn_column_x(b, i + 2, par)
                else:
                    turn_row_x(b, i + 2 - UNITS, par)

            def start_rows(b):
                u = unit_of_rows(b, 0)
                mix(u, 0, 0)
                turn_probs(u + 1, 1)
                mix(u, 1, 0)
                for j in range(LINES):
                    mix(u + 1, j, 1)

            def row_group(b, g, more, project, feed):
                group = b * GROUPS + g
                u = unit_of_rows(b, g * 2)
                pe.wait_ge(out_done, past(group * KT))
                if project:
                    pe.wait_ge(x_in, past((b * FEEDS + g - 2) * 16 + 16))
                    make_qk(g - 2, qk_ps)
                values(group, 0)
                if more:
                    scores(u + 2)
                if project:
                    pe.wait_ge(qk_out, past(group + (GROUPS - 1)))
                values(group, 1)
                if more:
                    turn_probs(u + 2, 0)
                    scores(u + 3)
                    turn_row_x(b, g * 2 + 2, 0)
                values(group, 2)
                if more:
                    mix(u + 2, 0, 0)
                    turn_row_x(b, g * 2 + 3, 1)
                    mix(u + 2, 1, 0)
                    turn_probs(u + 3, 0)
                values(group, 3)
                if more:
                    mix(u + 3, 0, 0)
                    mix(u + 3, 1, 0)

            def tail(b):
                for par in range(2):
                    pe.wait_ge(y_out[par], past(unit_of_columns(b + 1, 0)))
                pe.wait_ge(x_in, past((b + 1) * (FEEDS * 16)))
                make_qk(GROUPS - 2, qk_alone_ps[0])
                for half in range(2):
                    pe.wait_ge(x_line_in[half], past((b + 1) * LINE_LOADS * 16))
                    for k in range(KT):
                        mm = pe.matmul(qk_alone_ps[1][:, half * LINES * W:(half + 1) * LINES * W], wqk[:, k, :],
                                       x_line[:, half, k, :, :].rearrange("p j g -> p (j g)"),
                                       start=(k == 0), stop=(k == KT - 1))
                mm.then_inc(qk_done, 1)

            run(pe, first_image, start_columns, column_unit, start_rows, row_group, tail)

        @block.scalar
        def _(act):
            def take_qk(g, count, bank=qk_ps):
                act.wait_ge(qk_done, past(count + 1))
                act.activation(qk[:, row_pixels(g * ROWS, ROWS)], bank, ACT.Identity,
                               bias=bqk_col).then_inc(qk_out, 1)

            def take_turned_x(u, buf, mixed):
                act.wait_ge(mix_done, past(mixed))
                act.wait_ge(xt_done, past(u * 2 + 1))
                act.copy(x_turned[buf][:, 0, :], xt_ps[0][0:L, 0:C]).then_inc(xt_out[0], 1)

            def take_turned_probs(u, buf, mixed):
                act.wait_ge(mix_done, past(mixed))
                act.wait_ge(pt_done, past(u + 1))
                act.copy(probs_turned[buf][:, :, :], pt_ps).then_inc(pt_out, 1)

            def take_column(i, u):
                act.wait_ge(mix_done, past(u * 2 + 1))
                act.copy(column_of(i * LINES), y_ps_of(0)).then_inc(y_out[0], 1)

            def exps(u, par, buf, turned):
                act.wait_ge(pt_done, past(turned))
                act.wait_ge(max_done, past(u + 1))
                for j in range(LINES):
                    e = act.activation(probs[buf][:, j, :], score_ps[:, j, :], ACT.Exp,
                                       bias=neg_max[:, par, j:j + 1], accum_out=row_sum[:, par, j:j + 1])
                e.then_inc(exp_done, 1)

            def take_y_hi(g, u, group):
                act.wait_ge(y_out[1], past(u + 1))
                act.wait_ge(v_done, past(group * KT))
                act.copy(y_hi[:, :, 0:LINES * W], xy[:, :, row_pixels(g * ROWS, LINES)])\
                   .then_inc(y_hi_done[0], 1)
                act.wait_ge(y_out[0], past(u + 2))
                act.copy(y_hi[:, :, LINES * W:(LINES + 1) * W], xy[:, :, row_pixels(g * ROWS + LINES, 1)])\
                   .then_inc(y_hi_done[1], 1)

            def first_image():
                start_at_one(act, exp_done, pt_out, xt_out[0], y_out[0], y_hi_done[0],
                             y_hi_done[1], qk_out)
                act.wait_ge(small_in, 16 * 4)
                for par in range(2):
                    take_qk(par, par, qk_alone_ps[par])
                act.wait_ge(wv_in, 16)
                act.copy(wv_hi[:, :, :], wv_raw).then_inc(wv_hi_done, 1)
                with act.Fori(1, GROUPS // 2) as pair:
                    for par in range(2):
                        take_qk(pair * 2 + par, pair * 2 + par, qk_alone_ps[par])

            def start_columns(b):
                u = unit_of_columns(b, 0)
                exps(u, 0, 0, u)
                take_turned_x(u, 0, u * 2)
                take_turned_probs(u, 0, u * 2)
                exps(u + 1, 1, 1, u)
                take_turned_x(u + 1, 1, u * 2)

            def column_unit(b, i, par, left):
                u = unit_of_columns(b, i)
                take_turned_probs(u + 1, 1 - par, u * 2)
                take_column(i, u)
                exps(u + 2, par, par, u + 1)
                take_turned_x(u + 2, par, u * 2 + 1)

            def start_rows(b):
                u = unit_of_rows(b, 0)
                take_turned_probs(u + 1, 1, u * 2)
                act.wait_ge(mix_done, past(u * 2 + 4))

            def row_group(b, g, more, project, feed):
                group = b * GROUPS + g
                u = unit_of_rows(b, g * 2)
                take_y_hi(g, u, group)
                if project:
                    take_qk(g - 2, group + (GROUPS - 2))
                if more:
                    exps(u + 2, 0, 0, u + 2)
                    take_turned_probs(u + 2, 0, u * 2 + 4)
                    take_turned_x(u + 2, 0, u * 2 + 3)
                    exps(u + 3, 1, 0, u + 3)
                    take_turned_x(u + 3, 0, u * 2 + 5)
                    take_turned_probs(u + 3, 0, u * 2 + 6)

            def tail(b):
                for par in range(2):
                    g = GROUPS - 2 + par
                    take_qk(g, b * GROUPS + (GROUPS + g), qk_alone_ps[par])

            run(act, first_image, start_columns, column_unit, start_rows, row_group, tail)

        @block.vector
        def _(dve):
            def stage_k(i, u, rows):
                dve.wait_ge(scores_done, past(u))
                dve.tensor_copy(qk_line[:, 1, :, :], qk_lines(slice(CQK, P), rows, i)).then_inc(k_staged, 1)

            def stage_q(i, rows):
                dve.tensor_copy(qk_line[:, 0, :, :], qk_lines(slice(0, CQK), rows, i)).then_inc(q_staged, 1)

            def gather(i, par, turned):
                dve.wait_ge(xt_done, past(turned))
                dve.tensor_copy(x_line[:, par, :, :, :], columns_of(xy[:, :, :], i * LINES))\
                   .then_inc(x_gathered, 1)

            def row_max(u, par):
                dve.wait_ge(scores_done, past(u + 1))
                dve.tensor_reduce(neg_max[:, par, :], score_ps, AX_X, ALU.max, negate=True)\
                   .then_inc(max_done, 1)

            def divide(u, par, buf):
                dve.wait_ge(exp_done, past(u + 1))
                dve.reciprocal(row_inv[:, par, :], row_sum[:, par, :]).then_inc(inv_done, 1)
                dve.wait_ge(inv_done, past(u + 1))
                for j in range(LINES):
                    d = dve.tensor_scalar(probs[buf][:, j, :], probs[buf][:, j, :], row_inv[:, par, j:j + 1],
                                          None, ALU.mult)
                d.then_inc(probs_done, 1)

            def take_turned_x(u, buf, mixed):
                dve.wait_ge(mix_done, past(mixed))
                dve.wait_ge(xt_done, past(u * 2 + 2))
                dve.tensor_copy(x_turned[buf][:, 1, :], xt_ps[1][0:L, 0:C]).then_inc(xt_out[1], 1)

            def take_column(i, u):
                dve.wait_ge(mix_done, past(u * 2 + 2))
                dve.tensor_copy(column_of(i * LINES + 1), y_ps_of(1)).then_inc(y_out[1], 1)

            def add_row(i, u, j):
                row = xy[:, :, row_pixels(i * LINES + j, 1)]
                dve.wait_ge(mix_done, past(u * 2 + (j + 1)))
                dve.tensor_tensor(row, y_ps_of(j), row, ALU.add).then_inc(y_out[j], 1)

            def add_last_row(i, u):
                row = xy[:, :, row_pixels(i * LINES + 1, 1)]
                dve.wait_ge(mix_done, past(u * 2 + 2))
                dve.tensor_tensor(y_hi[:, :, GP - W:GP], y_ps_of(1), row, ALU.add).then_inc(y_hi_done[2], 1)
                dve.tensor_tensor(row, y_ps_of(1), row, ALU.add).then_inc(y_out[1], 1)

            def take_y_lo(g, u, group):
                dve.wait_ge(y_hi_done[1], past(group + 1))
                dve.wait_ge(y_hi_done[2], past(group + 1))
                dve.wait_ge(y_out[1], past(u + 1))
                part = slice(LINES * W, ROWS * W)
                dve.tensor_tensor(y_lo[:, :, part], xy[:, :, row_pixels(g * ROWS + LINES, LINES)],
                                  y_hi[:, :, part].bitcast(F32), ALU.subtract).then_inc(y_lo_done[1], 1)

            def take_output(g, group, m):
                if m == 0:
                    dve.wait_ge(rest_done, past(group * 2 + 2))
                dve.wait_ge(v_done, past(group * KT + (m + 1)))
                rest = xy[:, m, row_pixels(g * ROWS, ROWS)]
                dve.scalar_tensor_tensor(out=rest, in0=v_ps[m % 2][:, 0:GP], scalar=gamma_col, in1=rest,
                                         op0=ALU.mult, op1=ALU.add).then_inc(out_done, 1)

            def first_image():
                start_at_one(dve, k_staged, x_gathered, max_done, inv_done, probs_done, xt_out[1], y_out[1],
                             y_hi_done[2], y_lo_done[1], out_done, x_whole)
                dve.wait_ge(small_in, 16 * 4)
                dve.tensor_scalar(bias_col, bv_col, gamma_col, 2.0, ALU.mult, ALU.mult).then_inc(bias_done, 1)
                dve.wait_ge(wv_hi_done, 1)
                dve.tensor_tensor(wv_lo[:, :, :], wv_raw, wv_hi[:, :, :].bitcast(F32), ALU.subtract)\
                   .then_inc(wv_split, 1)

            def start_columns(b):
                u = unit_of_columns(b, 0)
                dve.wait_ge(qk_out, past(b * GROUPS + GROUPS))
                stage_k(0, u, False)
                stage_q(0, False)
                dve.wait_ge(x_whole, past(b))
                gather(0, 0, u * 2)
                gather(1, 1, u * 2)
                for par in range(2):
                    row_max(u + par, par)
                    stage_k(par + 1, u + (par + 1), False)
                    divide(u + par, par, par)
                    take_turned_x(u + par, par, u * 2)
                gather(2, 0, u * 2 + 2)

            def column_unit(b, i, par, left):
                u = unit_of_columns(b, i)
                row_max(u + 2, par)
                if left > 3:
                    stage_k(i + 3, u + 3, False)
                    gather(i + 3, 1 - par, u * 2 + 4)
                elif left > 1:
                    stage_k(i + 3 - UNITS, u + 3, True)
                    stage_q(i + 3 - UNITS, True)
                take_column(i, u)
                divide(u + 2, par, par)
                take_turned_x(u + 2, par, u * 2 + 2)

            def start_rows(b):
                u = unit_of_rows(b, 0)
                for j in range(LINES):
                    dve.wait_ge(y_out[j], past(u))
                add_row(0, u, 0)
                add_row(0, u, 1)
                add_row(1, u + 1, 0)
                add_last_row(1, u + 1)

            def row_group(b, g, more, project, feed):
                group = b * GROUPS + g
                i = g * 2
                u = unit_of_rows(b, i)
                take_y_lo(g, u + 1, group)
                if more:
                    stage_k(i + 2, u + 2, True)
                    stage_q(i + 2, True)
                    row_max(u + 2, 0)
                take_output(g, group, 0)
                if more:
                    stage_k(i + 3, u + 3, True)
                    stage_q(i + 3, True)
                    divide(u + 2, 0, 0)
                take_output(g, group, 1)
                if more:
                    row_max(u + 3, 1)
                    take_turned_x(u + 2, 0, u * 2 + 4)
                    divide(u + 3, 1, 0)
                take_output(g, group, 2)
                if more:
                    add_row(i + 2, u + 2, 0)
                    take_turned_x(u + 3, 0, u * 2 + 6)
                    add_row(i + 2, u + 2, 1)
                take_output(g, group, 3)
                if more:
                    add_row(i + 3, u + 3, 0)
                    add_last_row(i + 3, u + 3)

            def tail(b):
                dve.wait_ge(out_stored, past((b + 1) * (GROUPS * 16 * KT)))
                for half in range(2):
                    dve.wait_ge(x_line_in[half], past((b + 1) * LINE_LOADS * 16))
                    c = dve.tensor_copy(xy[:, :, row_pixels((GROUPS - 1) * ROWS + half * LINES, LINES)],
                                        x_line[:, half, :, :, :].rearrange("p k j g -> p k (j g)"))
                c.then_inc(x_whole, 1)

            run(dve, first_image, start_columns, column_unit, start_rows, row_group, tail)

        @block.gpsimd
        def _(pool):
            def wait_alone(semaphore, value):
                pool.wait_ge(semaphore, value).then_inc(pool_waited, 1)

            def stage_column_q(i, u):
                wait_alone(scores_done, past(u))
                pool.tensor_copy(qk_line[:, 0, :, :], qk_lines(slice(0, CQK), False, i)).then_inc(q_staged, 1)

            def take_y_lo(g, group):
                wait_alone(y_hi_done[0], past(group + 1))
                pool.tensor_tensor(y_lo[:, :, 0:LINES * W], xy[:, :, row_pixels(g * ROWS, LINES)],
                                   y_hi[:, :, 0:LINES * W].bitcast(F32), ALU.subtract).then_inc(y_lo_done[0], 1)

            def rest(g, group, half):
                wait_alone(y_lo_done[half], past(group + 1))
                pool.tensor_tensor(xy[:, :, row_pixels(g * ROWS + half * LINES, LINES)],
                                   x_line[:, half, :, :, :].rearrange("p k j g -> p k (j g)"),
                                   bias_col.rearrange("p (k o) -> p k o", o=1)
                                   .to_broadcast([P, KT, LINES * W]), ALU.add).then_inc(rest_done, 1)

            def first_image():
                start_at_one(pool, q_staged, y_lo_done[0], rest_done)
                pool.memset(ident[:, :], 0.0).then_inc(ident_zero, 1)
                pool.wait_ge(ident_zero, 1)
                pool.affine_select(out=ident[:, :], in_=ident[:, :], compare_op=ALU.not_equal, fill=1.0,
                                   base=0, pattern=[[-1, P]], channel_multiplier=1).then_inc(ident_done, 1)
                pool.wait_ge(bias_done, 1)

            def start_columns(b):
                u = unit_of_columns(b, 0)
                wait_alone(qk_out, past(b * GROUPS + GROUPS))
                for n in range(1, 3):
                    stage_column_q(n, u + n)

            def column_unit(b, i, par, left):
                if left > 3:
                    stage_column_q(i + 3, unit_of_columns(b, i + 3))

            def start_rows(b):
                pass

            def row_group(b, g, more, project, feed):
                take_y_lo(g, b * GROUPS + g)
                for half in range(2):
                    rest(g, b * GROUPS + g, half)

            def tail(b):
                pass

            run(pool, first_image, start_columns, column_unit, start_rows, row_group, tail)


def kernel(x, L0_conv_wq, L0_conv_bq, L0_conv_wk, L0_conv_bk, L0_conv_wv, L0_conv_bv, L0_conv_gamma):
    import numpy as np
    import concourse.bacc as bacc
    from concourse.bass_utils import run_bass_kernel_spmd

    x = np.ascontiguousarray(x)
    C = x.shape[1]
    arrays = {
        "x": x,
        "wqk_t": np.ascontiguousarray(np.concatenate([L0_conv_wq, L0_conv_wk]).T),
        "bqk": np.concatenate([L0_conv_bq, L0_conv_bk]).reshape(P, 1),
        "wv_t": np.ascontiguousarray(np.asarray(L0_conv_wv).T),
        "bv": np.ascontiguousarray(np.asarray(L0_conv_bv).reshape(C // P, P).T),
        "gamma": np.asarray(L0_conv_gamma).reshape(1, 1),
    }
    nc = bacc.Bacc("TRN2", target_bir_lowering=False, num_devices=1, dynamic_dma_scratch_size=64)
    args = [nc.dram_tensor(n, a.shape, mybir.dt.from_np(a.dtype), kind="ExternalInput").ap()
            for n, a in arrays.items()]
    out = nc.dram_tensor("out", x.shape, F32, kind="ExternalOutput").ap()
    build(nc, *args, out)
    r = run_bass_kernel_spmd(nc, [arrays], core_ids=[0])
    return r.results[0]["out"]
```
